# Optimizing a Trainium2 kernel written in Bass

```python
import numpy as np
import jax
import jax.numpy as jnp

def _softmax(x, axis=-1):
    return jax.nn.softmax(x, axis=axis)

def _gelu(x):
    return jax.nn.gelu(x, approximate=True)

def _silu(x):
    return jax.nn.silu(x)

def _sigmoid(x):
    return jax.nn.sigmoid(x)

def _layernorm(x, axis=-1, eps=1e-05):
    m = jnp.mean(x, axis=axis, keepdims=True)
    v = jnp.var(x, axis=axis, keepdims=True)
    return (x - m) / jnp.sqrt(v + eps)

def _scatter_add(tgt, idx, src, axis=0):
    return tgt.at[idx].add(src)

def _segment_sum(src, seg, n):
    return jax.ops.segment_sum(src, seg, n)
kernel_name = 'mk_dlrm_tower_d1_rec_r8_8edde9'

def setup_inputs(seed: int=0):
    np.random.seed(seed)
    _w = jnp.asarray

    def _rec_inputs():
        import jax
        import jax.numpy as jnp
        _tk = jax.random.key(seed)
        ids = jnp.stack([jax.random.randint(jax.random.fold_in(_tk, 200 + f), (2048,), 0, v, jnp.int32) for f, v in enumerate([1250, 125000, 12500, 1000, 1000, 12500, 1250, 12500, 12500, 1000, 1250, 1000, 1250, 1250, 12500, 12500, 1250, 1000, 1000, 1000, 1000, 12500, 1000, 1250, 1000, 1250, 1250])], axis=1)
        tbl_0 = 0.05 * jax.random.normal(jax.random.fold_in(_tk, 500 + 0), (1250, 128), jnp.float32)
        tbl_1 = 0.05 * jax.random.normal(jax.random.fold_in(_tk, 500 + 1), (125000, 128), jnp.float32)
        tbl_2 = 0.05 * jax.random.normal(jax.random.fold_in(_tk, 500 + 2), (12500, 128), jnp.float32)
        tbl_3 = 0.05 * jax.random.normal(jax.random.fold_in(_tk, 500 + 3), (1000, 128), jnp.float32)
        tbl_4 = 0.05 * jax.random.normal(jax.random.fold_in(_tk, 500 + 4), (1000, 128), jnp.float32)
        tbl_5 = 0.05 * jax.random.normal(jax.random.fold_in(_tk, 500 + 5), (12500, 128), jnp.float32)
        tbl_6 = 0.05 * jax.random.normal(jax.random.fold_in(_tk, 500 + 6), (1250, 128), jnp.float32)
        tbl_7 = 0.05 * jax.random.normal(jax.random.fold_in(_tk, 500 + 7), (12500, 128), jnp.float32)
        tbl_8 = 0.05 * jax.random.normal(jax.random.fold_in(_tk, 500 + 8), (12500, 128), jnp.float32)
        tbl_9 = 0.05 * jax.random.normal(jax.random.fold_in(_tk, 500 + 9), (1000, 128), jnp.float32)
        tbl_10 = 0.05 * jax.random.normal(jax.random.fold_in(_tk, 500 + 10), (1250, 128), jnp.float32)
        tbl_11 = 0.05 * jax.random.normal(jax.random.fold_in(_tk, 500 + 11), (1000, 128), jnp.float32)
        tbl_12 = 0.05 * jax.random.normal(jax.random.fold_in(_tk, 500 + 12), (1250, 128), jnp.float32)
        tbl_13 = 0.05 * jax.random.normal(jax.random.fold_in(_tk, 500 + 13), (1250, 128), jnp.float32)
        tbl_14 = 0.05 * jax.random.normal(jax.random.fold_in(_tk, 500 + 14), (12500, 128), jnp.float32)
        tbl_15 = 0.05 * jax.random.normal(jax.random.fold_in(_tk, 500 + 15), (12500, 128), jnp.float32)
        tbl_16 = 0.05 * jax.random.normal(jax.random.fold_in(_tk, 500 + 16), (1250, 128), jnp.float32)
        tbl_17 = 0.05 * jax.random.normal(jax.random.fold_in(_tk, 500 + 17), (1000, 128), jnp.float32)
        tbl_18 = 0.05 * jax.random.normal(jax.random.fold_in(_tk, 500 + 18), (1000, 128), jnp.float32)
        tbl_19 = 0.05 * jax.random.normal(jax.random.fold_in(_tk, 500 + 19), (1000, 128), jnp.float32)
        tbl_20 = 0.05 * jax.random.normal(jax.random.fold_in(_tk, 500 + 20), (1000, 128), jnp.float32)
        tbl_21 = 0.05 * jax.random.normal(jax.random.fold_in(_tk, 500 + 21), (12500, 128), jnp.float32)
        tbl_22 = 0.05 * jax.random.normal(jax.random.fold_in(_tk, 500 + 22), (1000, 128), jnp.float32)
        tbl_23 = 0.05 * jax.random.normal(jax.random.fold_in(_tk, 500 + 23), (1250, 128), jnp.float32)
        tbl_24 = 0.05 * jax.random.normal(jax.random.fold_in(_tk, 500 + 24), (1000, 128), jnp.float32)
        tbl_25 = 0.05 * jax.random.normal(jax.random.fold_in(_tk, 500 + 25), (1250, 128), jnp.float32)
        tbl_26 = 0.05 * jax.random.normal(jax.random.fold_in(_tk, 500 + 26), (1250, 128), jnp.float32)
        _rk = jax.random.fold_in(_tk, 7)
        r_bottom_mlp_out = 4.13588e-05 + 0.999923 * jax.random.normal(jax.random.fold_in(_rk, 101), (2048, 128), jnp.float32)
        W_top1 = 0.0405887 * jax.random.normal(jax.random.fold_in(_tk, 801), (607, 512), jnp.float32)
        W_top2 = 0.0441942 * jax.random.normal(jax.random.fold_in(_tk, 802), (512, 256), jnp.float32)
        W_top3 = 0.0625 * jax.random.normal(jax.random.fold_in(_tk, 803), (256, 1), jnp.float32)
        b_top1 = jnp.zeros((512,), jnp.float32)
        b_top2 = jnp.zeros((256,), jnp.float32)
        return (r_bottom_mlp_out, ids, tbl_0, tbl_1, tbl_2, tbl_3, tbl_4, tbl_5, tbl_6, tbl_7, tbl_8, tbl_9, tbl_10, tbl_11, tbl_12, tbl_13, tbl_14, tbl_15, tbl_16, tbl_17, tbl_18, tbl_19, tbl_20, tbl_21, tbl_22, tbl_23, tbl_24, tbl_25, tbl_26, W_top1, b_top1, W_top2, b_top2, W_top3)
    r_bottom_mlp_out, ids, tbl_0, tbl_1, tbl_2, tbl_3, tbl_4, tbl_5, tbl_6, tbl_7, tbl_8, tbl_9, tbl_10, tbl_11, tbl_12, tbl_13, tbl_14, tbl_15, tbl_16, tbl_17, tbl_18, tbl_19, tbl_20, tbl_21, tbl_22, tbl_23, tbl_24, tbl_25, tbl_26, W_top1, b_top1, W_top2, b_top2, W_top3 = _rec_inputs()

    def _L0_rec_setup():
        import jax, jax.numpy as jnp
        import numpy as np
        NUM_FEATURES = 27

        def _tril_indices(F):
            idx = []
            for i in range(F):
                for j in range(i):
                    idx.append(i * F + j)
            return np.asarray(idx, dtype=np.int32)
        TRIL_IDX = _tril_indices(NUM_FEATURES)
        key = jax.random.key(seed)
        k1, k2 = jax.random.split(key)
        B, F, D = (8192, NUM_FEATURES, 128)
        features = jax.random.normal(k1, (B, F, D), dtype=jnp.float32)
        bottom_mlp_out = jax.random.normal(k2, (B, D), dtype=jnp.float32)
        return {'features': features, 'bottom_mlp_out': bottom_mlp_out}
    _L0_rec_all = _L0_rec_setup()
    _L0_rec_in = {k: v for k, v in _L0_rec_all.items() if k in ()}
    del _L0_rec_all
    return {'r_bottom_mlp_out': r_bottom_mlp_out, 'ids': ids, 'tbl_0': tbl_0, 'tbl_1': tbl_1, 'tbl_2': tbl_2, 'tbl_3': tbl_3, 'tbl_4': tbl_4, 'tbl_5': tbl_5, 'tbl_6': tbl_6, 'tbl_7': tbl_7, 'tbl_8': tbl_8, 'tbl_9': tbl_9, 'tbl_10': tbl_10, 'tbl_11': tbl_11, 'tbl_12': tbl_12, 'tbl_13': tbl_13, 'tbl_14': tbl_14, 'tbl_15': tbl_15, 'tbl_16': tbl_16, 'tbl_17': tbl_17, 'tbl_18': tbl_18, 'tbl_19': tbl_19, 'tbl_20': tbl_20, 'tbl_21': tbl_21, 'tbl_22': tbl_22, 'tbl_23': tbl_23, 'tbl_24': tbl_24, 'tbl_25': tbl_25, 'tbl_26': tbl_26, 'W_top1': W_top1, 'b_top1': b_top1, 'W_top2': W_top2, 'b_top2': b_top2, 'W_top3': W_top3}

def reference(r_bottom_mlp_out, ids, tbl_0, tbl_1, tbl_2, tbl_3, tbl_4, tbl_5, tbl_6, tbl_7, tbl_8, tbl_9, tbl_10, tbl_11, tbl_12, tbl_13, tbl_14, tbl_15, tbl_16, tbl_17, tbl_18, tbl_19, tbl_20, tbl_21, tbl_22, tbl_23, tbl_24, tbl_25, tbl_26, W_top1, b_top1, W_top2, b_top2, W_top3):
    import jax
    import jax.numpy as jnp

    def _L0_rec_ref(features, bottom_mlp_out):
        import jax, jax.numpy as jnp
        import numpy as np
        NUM_FEATURES = 27

        def _tril_indices(F):
            idx = []
            for i in range(F):
                for j in range(i):
                    idx.append(i * F + j)
            return np.asarray(idx, dtype=np.int32)
        TRIL_IDX = _tril_indices(NUM_FEATURES)
        B = features.shape[0]
        F = features.shape[1]
        interactions = jnp.einsum('bfd,bgd->bfg', features, features)
        interactions = interactions.reshape(B, F * F)
        x = interactions[:, TRIL_IDX]
        return jnp.concatenate([bottom_mlp_out, x], axis=1)
    e = jnp.stack([tbl_0[ids[:, 0]], tbl_1[ids[:, 1]], tbl_2[ids[:, 2]], tbl_3[ids[:, 3]], tbl_4[ids[:, 4]], tbl_5[ids[:, 5]], tbl_6[ids[:, 6]], tbl_7[ids[:, 7]], tbl_8[ids[:, 8]], tbl_9[ids[:, 9]], tbl_10[ids[:, 10]], tbl_11[ids[:, 11]], tbl_12[ids[:, 12]], tbl_13[ids[:, 13]], tbl_14[ids[:, 14]], tbl_15[ids[:, 15]], tbl_16[ids[:, 16]], tbl_17[ids[:, 17]], tbl_18[ids[:, 18]], tbl_19[ids[:, 19]], tbl_20[ids[:, 20]], tbl_21[ids[:, 21]], tbl_22[ids[:, 22]], tbl_23[ids[:, 23]], tbl_24[ids[:, 24]], tbl_25[ids[:, 25]], tbl_26[ids[:, 26]]], axis=1)
    z = _L0_rec_ref(e, r_bottom_mlp_out)
    z = z.reshape(z.shape[0], -1)
    h = jnp.concatenate([z, r_bottom_mlp_out], axis=1)
    h = jnp.maximum(h @ W_top1 + b_top1, 0.0)
    h = jnp.maximum(h @ W_top2 + b_top2, 0.0)
    y = h @ W_top3
    return y

_drawn_inputs = setup_inputs


def setup_inputs(seed=0):
    import zlib

    import numpy as np

    out = dict(_drawn_inputs(seed))
    spreads = {'b_top1': (0.0, 0.1), 'b_top2': (0.0, 0.1)}
    factors = {'tbl_0': 4.857,
     'tbl_1': 5.164,
     'tbl_2': 4.654,
     'tbl_3': 4.077,
     'tbl_4': 4.772,
     'tbl_5': 4.296,
     'tbl_6': 4.782,
     'tbl_7': 4.226,
     'tbl_8': 4.477,
     'tbl_9': 4.932,
     'tbl_10': 4.392,
     'tbl_11': 4.472,
     'tbl_12': 4.465,
     'tbl_13': 4.447,
     'tbl_14': 4.814,
     'tbl_15': 4.901,
     'tbl_16': 4.673,
     'tbl_17': 4.955,
     'tbl_18': 4.263,
     'tbl_19': 4.347,
     'tbl_20': 4.392,
     'tbl_21': 4.932,
     'tbl_22': 4.74,
     'tbl_23': 4.894,
     'tbl_24': 4.417,
     'tbl_25': 4.918,
     'tbl_26': 4.383}
    for name, (base, spread) in spreads.items():
        noise = np.random.default_rng([zlib.crc32(name.encode()), seed]).standard_normal(out[name].shape)
        drawn = base * np.exp(spread * noise) if base else spread * noise
        out[name] = jnp.asarray(drawn.astype(out[name].dtype))
    for name, factor in factors.items():
        out[name] = (out[name] * factor).astype(out[name].dtype)
    return out
```

```python
import concourse.bass as bass
from concourse import mybir
from contextlib import ExitStack

BATCH = 2048
DIM = 128
FEATURES = 27
ROWS = [1250, 125000, 12500, 1000, 1000, 12500, 1250, 12500, 12500, 1000, 1250, 1000, 1250, 1250,
        12500, 12500, 1250, 1000, 1000, 1000, 1000, 12500, 1000, 1250, 1000, 1250, 1250]
HIDDEN1, HIDDEN2 = 512, 256
STEP = 256
STEPS = BATCH // STEP
TILES = STEP // 128

NP = 7
PICK_ROWS, PICK_PART = 1000, 125
PICK_CHUNKS = PICK_ROWS // PICK_PART
PICKED = [f for f in range(FEATURES) if ROWS[f] == PICK_ROWS][:NP]
GATHERED = [f for f in range(FEATURES) if f not in PICKED]
SLOTS = GATHERED + PICKED
NG = len(GATHERED)
HALVES = 2

SLOT_PAD = 32
QUADS = 4
PROD_ROWS = (QUADS - 1) * SLOT_PAD + FEATURES
GROUPS = 128 // QUADS
GROUPS_PER_USE = 8
USES = GROUPS // GROUPS_PER_USE
COLS = TILES * GROUPS

SHIFTS = FEATURES // 2
WRAP = FEATURES + SHIFTS
CHUNKS = 3
SHIFTS_PER_CHUNK = 4
CUT = FEATURES // CHUNKS
PAIRS_PER_CHUNK = SHIFTS_PER_CHUNK * FEATURES + CUT
KC1 = 1 + CHUNKS
NC1, NC2 = HIDDEN1 // 128, HIDDEN2 // 128

TURN_WIDTH = 4
TURNS = -(-NG // TURN_WIDTH)
STAGES = 4

PICKS = [("pick", n, None) for n in range(NP)]
TURN = [[("turn", t * TURNS + n) for n in range(TURNS)] for t in range(TILES)]
PROD = [[("prod", t * USES + u) for u in range(USES)] for t in range(TILES)]
ALL = None


def mlp(tile):
    return ([("h1", n, tile) for n in range(NC1)], [("h2", n, tile) for n in range(NC2)], [("y", 0, tile)])


H1, H2, Y = mlp(ALL)
MLP = H1 + H2 + Y
LAST_MLP = [item for t in range(TILES) for part in mlp(t) for item in part]


def woven(a, b, lead):
    out, a, b = a[:lead], list(a[lead:]), list(b)
    while a or b:
        out = out + b[:1] + a[:1]
        a, b = a[1:], b[1:]
    return out


OPENING, INNER, CLOSING, AFTER = "opening", "inner", "closing", "after"
ORDER = {
    OPENING: woven(PICKS, TURN[0], 2) + PROD[0] + TURN[1] + PROD[1],
    INNER: (woven(PICKS, TURN[0], 2) + TURN[1][:1] + PROD[0] + woven(H1 + H2, TURN[1][1:], 1) + Y + PROD[1]),
    CLOSING: woven(PICKS, TURN[0], 2) + TURN[1][:1] + PROD[0] + TURN[1][1:] + H1[:1] + PROD[1] + H1[1:] + H2 + Y,
    AFTER: LAST_MLP,
}
SHARED = ("pick", "h1", "h2", "y")


def turn_width(q):
    return min(TURN_WIDTH, NG - TURN_WIDTH * (q % TURNS))


def shared_place(kind, item):
    return [x for x in ORDER[kind] if x[0] in SHARED].index(item)


def pair_rows():
    def row(i, k):
        a, b = SLOTS[i], SLOTS[(i + k) % FEATURES]
        hi, lo = max(a, b), min(a, b)
        return DIM + hi * (hi - 1) // 2 + lo
    rows = []
    for c in range(CHUNKS):
        for k in range(SHIFTS_PER_CHUNK * c + 1, SHIFTS_PER_CHUNK * (c + 1) + 1):
            rows += [row(i, k) for i in range(FEATURES)]
        rows += [row(i, SHIFTS) for i in range(CUT * c, CUT * (c + 1))]
    return rows


def build(nc, gather_ids, pick_ids, bottom_t, tables, w_bottom, w_pairs, b1, w2, b2, w3, out):
    fp32, f32r, i32 = mybir.dt.float32, mybir.dt.float32r, mybir.dt.int32
    ALU, ACT = mybir.AluOpType, mybir.ActivationFunctionType

    ctx = ExitStack()
    with ctx:
        def sb(name, shape, dt):
            return ctx.enter_context(nc.sbuf_tensor(name, shape, dt))

        def pb(name, shape, dt):
            return ctx.enter_context(nc.psum_tensor(name, shape, dt))

        def sem(name):
            return ctx.enter_context(nc.semaphore(name))

        gids_all = sb("gids_all", [128, STEPS, TILES * NG], i32)
        gids = [sb(f"gids{p}", [128, TILES * NG], i32) for p in range(2)]
        rows = sb("rows", [128, 2, TILES, NG * DIM], fp32)
        features = sb("features", [128, TILES, GROUPS, QUADS, SLOT_PAD], fp32)
        pids = sb("pids", [128, NP, STEP], i32)
        onehot = sb("onehot", [128, 2, PICK_CHUNKS, STEP], f32r)
        halves = sb("halves", [128, NP, HALVES, PICK_CHUNKS * DIM], f32r)
        products = sb("products", [128, FEATURES, COLS], fp32)
        pair_cols = sb("pair_cols", [128, 2, CHUNKS, STEP], fp32)
        bottom = sb("bottom", [128, 2, STEP], fp32)
        w1_sb = sb("w1_sb", [128, KC1, HIDDEN1], fp32)
        w2_sb = sb("w2_sb", [128, NC1, HIDDEN2], fp32)
        w3_sb = sb("w3_sb", [128, NC2], fp32)
        b1_sb = sb("b1_sb", [128, NC1], fp32)
        b2_sb = sb("b2_sb", [128, NC2], fp32)
        hid1 = sb("hid1", [128, NC1, STEP], fp32)
        hid2 = sb("hid2", [128, NC2, STEP], fp32)
        y_sb = sb("y_sb", [1, STEP], fp32)
        ident = sb("ident", [128, 128], fp32)
        row_id_i = sb("row_id_i", [128, PICK_CHUNKS], i32)
        row_id = sb("row_id", [128, PICK_CHUNKS], fp32)

        table_size = PICK_CHUNKS * DIM
        staged = [rows[0:PICK_PART, 1, n // 2, n % 2 * table_size:(n % 2 + 1) * table_size] for n in range(STAGES)]
        w1_again = hid1[:, 0:HIDDEN1 // STEP, :].rearrange("p a b -> p (a b)")

        turned = [pb(f"turned{n}", [128, TURN_WIDTH, 128], fp32) for n in range(2)]
        prods = [pb(f"prods{n}", [128, GROUPS_PER_USE, 128], fp32) for n in range(2)]
        shared = [pb(f"shared{n}", [128, 512], fp32) for n in range(2)]

        scratch = nc.dram_tensor("scratch", (128, WRAP, COLS), fp32, kind="Internal").ap()

        gids_loaded = sem("gids_loaded")
        gids_copied = sem("gids_copied")
        carried = sem("carried")
        pids_loaded = sem("pids_loaded")
        bottom_loaded = sem("bottom_loaded")
        table_loaded = [sem(f"table_loaded{n}") for n in range(STAGES)]
        weights_loaded = sem("weights_loaded")
        w1_ready = sem("w1_ready")
        ident_zero = sem("ident_zero")
        ident_ready = sem("ident_ready")
        iota_ready = sem("iota_ready")
        consts_ready = sem("consts_ready")
        padded = sem("padded")
        high_ready = sem("high_ready")
        low_ready = sem("low_ready")
        gathered = [[sem(f"gathered{p}{q}") for q in range(TILES * TURNS)] for p in range(2)]
        onehot_ready = sem("onehot_ready")
        shared_full = sem("shared_full")
        shared_free = sem("shared_free")
        turned_full = sem("turned_full")
        turned_free = sem("turned_free")
        prods_full = sem("prods_full")
        prods_free = sem("prods_free")
        scratch_written = sem("scratch_written")
        pairs_loaded = sem("pairs_loaded")
        y_stored = sem("y_stored")

        def of_tile(cols, tile):
            if tile is ALL:
                return cols
            return cols.rearrange("d (g t m) -> d g t m", g=QUADS, t=TILES)[:, :, tile, :]

        PAIR_LOADS = CHUNKS * (SHIFTS_PER_CHUNK + 1)
        WEIGHT_LOADS = 7

        def first(s):
            return type(s) is int and s == 0

        def shared_before(s):
            return 0 if first(s) else s * (NP + len(MLP)) - len(MLP)

        def shared_bank(s, par, place):
            return shared[place % 2 if first(s) else (par * (NP + len(MLP)) + len(MLP) + place) % 2]

        def run_steps(engine, body):
            body(0, 0, OPENING)
            with engine.Fori(0, (STEPS - 2) // 2) as i:
                body(i * 2 + 1, 1, INNER)
                body(i * 2 + 2, 0, INNER)
            body(STEPS - 1, 1, CLOSING)

        block = ctx.enter_context(nc.Block())

        @block.gpsimd
        def _(pool):
            nc.gpsimd.memset(ident[:, :], 0.0).then_inc(ident_zero, 1)
            nc.gpsimd.iota(row_id_i[:, :], pattern=[[1, PICK_CHUNKS]], base=0,
                           channel_multiplier=PICK_CHUNKS).then_inc(iota_ready, 1)
            pool.wait_ge(ident_zero, 1)
            nc.gpsimd.affine_select(out=ident[:, :], in_=ident[:, :], compare_op=ALU.not_equal, fill=1.0,
                                    base=0, pattern=[[-1, 128]], channel_multiplier=1).then_inc(ident_ready, 1)
            pool.wait_ge(gids_loaded, 16)
            nc.gpsimd.tensor_copy(gids[0][:, :], gids_all[:, 0, :]).then_inc(gids_copied, 1)

            def step(s, par, k, last=False):
                pool.wait_ge(gids_copied, s + 1)
                pool.sem_inc(carried, 1)
                for t in range(TILES):
                    if not k_is_0(k):
                        pool.wait_ge(turned_full, (s - 2) * (TILES * TURNS) + (t + 1) * TURNS)
                        pool.sem_inc(carried, 1)
                    elif par == 1:
                        pool.wait_ge(low_ready, NP)
                    for g, f in enumerate(GATHERED):
                        pool.indirect_dma_start(
                            rows[:, par, t, g * DIM:(g + 1) * DIM], None, tables[f][:, :],
                            bass.IndirectOffsetOnAxis(ap=gids[par][:, t * NG + g:t * NG + g + 1], axis=0),
                        ).then_inc(gathered[par][t * TURNS + g // TURN_WIDTH], 16)
                    if t == 0 and not last:
                        if not (k_is_0(k) and par == 0):
                            for q in range(TILES * TURNS):
                                pool.wait_ge(gathered[1 - par][q], 16 * turn_width(q) * (k + par))
                            pool.sem_inc(carried, 1)
                        nc.gpsimd.tensor_copy(gids[1 - par][:, :], gids_all[:, s + 1, :]).then_inc(gids_copied, 1)

            def k_is_0(k):
                return type(k) is int and k == 0

            step(0, 0, 0)
            step(1, 1, 0)
            with pool.Fori(1, STEPS // 2 - 1) as i:
                step(i * 2, 0, i)
                step(i * 2 + 1, 1, i)
            step(STEPS - 2, 0, STEPS // 2 - 1)
            step(STEPS - 1, 1, STEPS // 2 - 1, last=True)

        @block.sync
        def _(sp):
            def load_pids(s):
                sp.dma_start(pids[:, :, :], pick_ids[s, :, :].partition_broadcast(128)).then_inc(pids_loaded, 16)

            def load_bottom(s, par):
                sp.dma_start(bottom[:, par, :], bottom_t[s, :, :]).then_inc(bottom_loaded, 16)

            def store_y(s):
                sp.dma_start(out[s, :, :], y_sb[:, :]).then_inc(y_stored, 16)

            def finish_y(s, kind):
                sp.wait_ge(shared_free, shared_before(s) + shared_place(kind, Y[0]) + 1)
                store_y(s - 1)
                sp.wait_ge(y_stored, s * 16)

            sp.dma_start(gids_all[:, :, :], gather_ids[:, :, :]).then_inc(gids_loaded, 16)
            load_pids(0)
            for n, f in enumerate(PICKED):
                if n >= STAGES:
                    sp.wait_ge(low_ready, n - STAGES + 1)
                sp.dma_start(staged[n % STAGES], tables[f].rearrange("(p c) d -> p (c d)", p=PICK_PART)
                             ).then_inc(table_loaded[n % STAGES], 16)

            def relayout(s, par, tiles=range(TILES)):
                t0, n_tiles = tiles[0], len(tiles)
                cols = slice(t0 * GROUPS, (t0 + n_tiles) * GROUPS)
                sp.wait_ge(prods_free, s * (TILES * USES) + (t0 + n_tiles) * USES)
                if type(s) is int and s == STEPS - 1:
                    sp.wait_ge(pairs_loaded, s * (16 * PAIR_LOADS) + 16 * PAIR_LOADS * t0)
                sp.dma_start(scratch[:, 0:FEATURES, cols], products[:, :, cols]).then_inc(scratch_written, 16)
                sp.dma_start(scratch[:, FEATURES:WRAP, cols], products[:, 0:SHIFTS, cols]).then_inc(scratch_written, 16)
                sp.wait_ge(scratch_written, s * 32 + 32 * (t0 + 1))
                by_quad = scratch.rearrange("(g i) j m -> g (i j m)", g=QUADS)
                one_on = (WRAP + 1) * COLS

                def diagonal(c, part, shift, i0, n):
                    start = i0 * one_on + shift * COLS
                    src = by_quad[:, start:start + n * one_on].rearrange("g (i x) -> i g x", i=n)[:, :, cols]
                    dst = pair_cols[part:part + n, par, c, :].rearrange("q (g m) -> q g m", g=QUADS)[:, :, cols]
                    sp.dma_start(dst, src).then_inc(pairs_loaded, 16)

                for c in range(CHUNKS):
                    for r in range(SHIFTS_PER_CHUNK):
                        diagonal(c, r * FEATURES, SHIFTS_PER_CHUNK * c + r + 1, 0, FEATURES)
                    diagonal(c, SHIFTS_PER_CHUNK * FEATURES, SHIFTS, CUT * c, CUT)

            def step(s, par, kind):
                if kind != CLOSING:
                    sp.wait_ge(onehot_ready, s * NP + NP)
                    load_pids(s + 1)
                load_bottom(s, par)
                if kind == INNER:
                    finish_y(s, kind)
                if kind != CLOSING:
                    relayout(s, par)
                else:
                    relayout(s, par, [0])
                    relayout(s, par, [1])
                    finish_y(s, kind)

            run_steps(sp, step)
            sp.wait_ge(shared_free, shared_before(STEPS) + len(LAST_MLP))
            store_y(STEPS - 1)
            sp.wait_ge(y_stored, 16 * STEPS)

        @block.scalar
        def _(act):
            act.dma_start(w1_sb[:, 0, :], w_bottom[0, :, :]).then_inc(weights_loaded, 16)
            act.dma_start(w1_again, w_bottom[1, :, :]).then_inc(weights_loaded, 16)
            act.dma_start(w1_sb[0:PAIRS_PER_CHUNK, 1:KC1, :],
                          w_pairs.rearrange("c q n -> q c n")).then_inc(weights_loaded, 16)
            act.dma_start(w2_sb[:, :, :], w2.rearrange("(c p) n -> p c n", p=128)).then_inc(weights_loaded, 16)
            act.dma_start(w3_sb[:, :], w3[:, :]).then_inc(weights_loaded, 16)
            act.dma_start(b1_sb[:, :], b1[:, :]).then_inc(weights_loaded, 16)
            act.dma_start(b2_sb[:, :], b2[:, :]).then_inc(weights_loaded, 16)

            def high_half(n):
                act.wait_ge(table_loaded[n % STAGES], 16 * (n // STAGES + 1))
                nc.scalar.copy(halves[0:PICK_PART, n, 0, :], staged[n % STAGES]).then_inc(high_ready, 1)
            for n in range(STAGES):
                high_half(n)

            def copy_shared(s, par, kind, item):
                what, n, tile = item
                place = shared_place(kind, item)
                src = shared_bank(s, par, place)[:, 0:STEP if tile is ALL else 128]
                act.wait_ge(shared_full, shared_before(s) + place + 1)
                if item == H1[0]:
                    act.wait_ge(w1_ready, 1)
                if what == "pick":
                    ins = nc.scalar.copy(features[:, :, :, :, NG + n].rearrange("d t m g -> d g t m"),
                                         src.rearrange("d (g t m) -> d g t m", g=QUADS, t=TILES))
                elif what == "h1":
                    ins = nc.scalar.activation(of_tile(hid1[:, n, :], tile), src, ACT.Relu, bias=b1_sb[:, n:n + 1])
                elif what == "h2":
                    ins = nc.scalar.activation(of_tile(hid2[:, n, :], tile), src, ACT.Relu, bias=b2_sb[:, n:n + 1])
                else:
                    if kind == AFTER:
                        act.wait_ge(y_stored, 16 * (STEPS - 1))
                    ins = nc.scalar.copy(of_tile(y_sb[0:1, :], tile), src[0:1, :])
                ins.then_inc(shared_free, 1)

            def copy_turned(s, q):
                t, n = divmod(q, TURNS)
                act.wait_ge(turned_full, s * (TILES * TURNS) + q + 1)
                width = turn_width(q)
                dst = features[:, t, :, :, TURN_WIDTH * n:TURN_WIDTH * n + width].rearrange("d m g f -> d g m f")
                nc.scalar.copy(dst, turned[q % 2][:, 0:width, :].rearrange("d f (g m) -> d g m f", g=QUADS)
                               ).then_inc(turned_free, 1)

            def copy_products(s, q):
                t, u = divmod(q, USES)
                if q == 0 and first(s):
                    act.wait_ge(padded, 1)
                elif q == 0:
                    act.wait_ge(scratch_written, s * 32)
                act.wait_ge(prods_full, s * (TILES * USES) + q + 1)
                m0 = t * GROUPS + GROUPS_PER_USE * u
                for g in range(QUADS):
                    quad = slice(SLOT_PAD * g, min(SLOT_PAD * (g + 1), PROD_ROWS))
                    last = nc.scalar.copy(products[quad, :, m0:m0 + GROUPS_PER_USE].rearrange("p j m -> p m j"),
                                          prods[q % 2][quad, :, FEATURES * g:FEATURES * (g + 1)])
                last.then_inc(prods_free, 1)

            def step(s, par, kind):
                for item in ORDER[kind]:
                    if item[0] == "turn":
                        copy_turned(s, item[1])
                    elif item[0] == "prod":
                        copy_products(s, item[1])
                    else:
                        if kind == OPENING and item[1] + STAGES < NP:
                            high_half(item[1] + STAGES)
                        copy_shared(s, par, kind, item)

            run_steps(act, step)
            step(STEPS, 0, AFTER)

        @block.vector
        def _(dve):
            nc.vector.memset(features[:, :, :, :, FEATURES:SLOT_PAD], 0.0)
            nc.vector.memset(products[SLOT_PAD * (QUADS - 1):, :, :], 0.0).then_inc(padded, 1)
            dve.wait_ge(iota_ready, 1)
            nc.vector.tensor_copy(row_id[:, :], row_id_i[:, :]).then_inc(consts_ready, 1)
            dve.wait_ge(consts_ready, 1)

            def step(s, par, kind):
                dve.wait_ge(pids_loaded, s * 16 + 16)
                for n in range(NP):
                    if kind == OPENING:
                        dve.wait_ge(high_ready, n + 1)
                        nc.vector.tensor_tensor(halves[0:PICK_PART, n, 1, :], staged[n % STAGES],
                                                halves[0:PICK_PART, n, 0, :].bitcast(fp32),
                                                ALU.subtract).then_inc(low_ready, 1)
                    if n >= 2:
                        dve.wait_ge(shared_full, shared_before(s) + shared_place(kind, PICKS[n - 2]) + 1)
                    elif n == 0 and kind != OPENING:
                        dve.wait_ge(prods_full, (s - 1) * (TILES * USES) + 1)
                    for c in range(PICK_CHUNKS):
                        last = nc.vector.tensor_scalar(onehot[0:PICK_PART, (par * NP + n) % 2, c, :],
                                                       pids[0:PICK_PART, n, :],
                                                       row_id[0:PICK_PART, c:c + 1], None, ALU.is_equal)
                    last.then_inc(onehot_ready, 1)
                if kind == OPENING:
                    dve.wait_ge(weights_loaded, 16 * WEIGHT_LOADS)
                    nc.vector.tensor_tensor(w1_sb[:, 0, :], w1_sb[:, 0, :], w1_again, ALU.add).then_inc(w1_ready, 1)

            run_steps(dve, step)

        @block.tensor
        def _(pe):
            pe.wait_ge(ident_ready, 1)

            def pick(s, par, n, dst):
                pe.wait_ge(onehot_ready, s * NP + n + 1)
                if first(s):
                    pe.wait_ge(low_ready, n + 1)
                for half in range(HALVES):
                    for c in range(PICK_CHUNKS):
                        last = nc.tensor.matmul(dst, halves[0:PICK_PART, n, half, c * DIM:(c + 1) * DIM],
                                                onehot[0:PICK_PART, (par * NP + n) % 2, c, :],
                                                start=(half == 0 and c == 0),
                                                stop=(half == HALVES - 1 and c == PICK_CHUNKS - 1))
                return last

            def layer1(s, par, n, tile, dst):
                cols = slice(128 * n, 128 * n + 128)
                if n == 0:
                    pe.wait_ge(bottom_loaded, s * 16)
                    pe.wait_ge(w1_ready, 1)
                nc.tensor.matmul(dst, w1_sb[:, 0, cols], of_tile(bottom[:, par, :], tile), start=True, stop=False)
                if n == 0:
                    pe.wait_ge(pairs_loaded, s * (16 * PAIR_LOADS) + 16 * PAIR_LOADS * (tile or 0))
                for c in range(CHUNKS):
                    last = nc.tensor.matmul(dst, w1_sb[0:PAIRS_PER_CHUNK, 1 + c, cols],
                                            of_tile(pair_cols[0:PAIRS_PER_CHUNK, par, c, :], tile), start=False, stop=(c == CHUNKS - 1))
                return last

            def layer2(n, tile, dst):
                for c in range(NC1):
                    last = nc.tensor.matmul(dst, w2_sb[:, c, 128 * n:128 * n + 128],
                                            of_tile(hid1[:, c, :], tile),
                                            start=(c == 0), stop=(c == NC1 - 1))
                return last

            def layer3(tile, dst):
                for c in range(NC2):
                    last = nc.tensor.matmul(dst, w3_sb[:, c:c + 1], of_tile(hid2[:, c, :], tile),
                                            start=(c == 0), stop=(c == NC2 - 1))
                return last

            def fill_shared(s, par, kind, item):
                what, n, tile = item
                place = shared_place(kind, item)
                dst = shared_bank(s, par, place)[:, 0:STEP if tile is ALL else 128]
                if not (first(s) and place < 2):
                    pe.wait_ge(shared_free, shared_before(s) + place - 1)
                if what == "pick":
                    last = pick(s, par, n, dst)
                elif what == "h1":
                    last = layer1(s, 1 - par, n, tile, dst)
                elif what == "h2":
                    pe.wait_ge(shared_free, shared_before(s) + shared_place(kind, mlp(tile)[0][-1]) + 1)
                    last = layer2(n, tile, dst)
                else:
                    pe.wait_ge(shared_free, shared_before(s) + shared_place(kind, mlp(tile)[1][-1]) + 1)
                    last = layer3(tile, dst[0:1, :])
                last.then_inc(shared_full, 1)

            def transpose_rows(s, par, q):
                t, n = divmod(q, TURNS)
                pe.wait_ge(gathered[par][q], (s - par) * (8 * turn_width(q)) + 16 * turn_width(q))
                if not (first(s) and q < 2):
                    pe.wait_ge(turned_free, s * (TILES * TURNS) + q - 1)
                for j in range(turn_width(q)):
                    g = TURN_WIDTH * n + j
                    last = nc.tensor.transpose(turned[q % 2][:, j, :], rows[:, par, t, g * DIM:(g + 1) * DIM],
                                               ident[:, :])
                last.then_inc(turned_full, 1)

            def pair_products(s, kind, q):
                t, u = divmod(q, USES)
                if u == 0:
                    pe.wait_ge(turned_free, s * (TILES * TURNS) + (t + 1) * TURNS)
                    if t == 0:
                        pe.wait_ge(shared_free, shared_before(s) + shared_place(kind, PICKS[-1]) + 1)
                if not (first(s) and q < 2):
                    pe.wait_ge(prods_free, s * (TILES * USES) + q - 1)
                for j in range(GROUPS_PER_USE):
                    group = features[:, t, GROUPS_PER_USE * u + j, :, :]
                    last = nc.tensor.matmul(prods[q % 2][0:PROD_ROWS, j, 0:QUADS * FEATURES], group.rearrange("d g f -> d (g f)")[:, 0:PROD_ROWS],
                                            group[:, :, 0:FEATURES], start=True, stop=True)
                last.then_inc(prods_full, 1)

            def step(s, par, kind):
                for item in ORDER[kind]:
                    if item[0] == "turn":
                        transpose_rows(s, par, item[1])
                    elif item[0] == "prod":
                        pair_products(s, kind, item[1])
                    else:
                        fill_shared(s, par, kind, item)

            run_steps(pe, step)
            step(STEPS, 0, AFTER)


def kernel(**inputs):
    import numpy as np
    import concourse.bacc as bacc
    from concourse.bass_utils import run_bass_kernel_spmd

    a = {name: np.asarray(x) for name, x in inputs.items()}
    ids, w1 = a["ids"], a["W_top1"]

    def in_product_order(x):
        return x.reshape(STEPS, TILES, QUADS, GROUPS, -1).transpose(0, 2, 1, 3, 4).reshape(STEPS, STEP, -1)

    laid = {
        "gather_ids": ids[:, GATHERED].reshape(STEPS, TILES, 128, NG).transpose(2, 0, 1, 3)
                      .reshape(128, STEPS, TILES * NG),
        "pick_ids": in_product_order(ids[:, PICKED]).transpose(0, 2, 1),
        "bottom_t": in_product_order(a["r_bottom_mlp_out"]).transpose(0, 2, 1),
        "w_bottom": np.stack([w1[:DIM], w1[-DIM:]]),
        "w_pairs": w1[pair_rows()].reshape(CHUNKS, PAIRS_PER_CHUNK, HIDDEN1),
        "b1": a["b_top1"].reshape(NC1, 128).T,
        "w2": a["W_top2"],
        "b2": a["b_top2"].reshape(NC2, 128).T,
        "w3": a["W_top3"].reshape(NC2, 128).T,
    }
    laid.update({f"tbl_{f}": a[f"tbl_{f}"] for f in range(FEATURES)})
    laid = {name: np.ascontiguousarray(x) for name, x in laid.items()}

    nc = bacc.Bacc("TRN2", target_bir_lowering=False, num_devices=1)
    ap = {name: nc.dram_tensor(f"in_{name}", x.shape, mybir.dt.from_np(x.dtype), kind="ExternalInput").ap()
          for name, x in laid.items()}
    out = nc.dram_tensor("out_y", (STEPS, 1, STEP), mybir.dt.float32, kind="ExternalOutput").ap()
    build(nc, ap["gather_ids"], ap["pick_ids"], ap["bottom_t"], [ap[f"tbl_{f}"] for f in range(FEATURES)],
          ap["w_bottom"], ap["w_pairs"], ap["b1"], ap["w2"], ap["b2"], ap["w3"], out)
    r = run_bass_kernel_spmd(nc, [{f"in_{name}": x for name, x in laid.items()}], core_ids=[0])
    y = r.results[0]["out_y"].reshape(STEPS, QUADS, TILES, GROUPS)
    return y.transpose(0, 2, 1, 3).reshape(BATCH, 1)
```

```python
import concourse.bass as bass
from concourse import mybir
from contextlib import ExitStack

BATCH = 2048
DIM = 128
FEATURES = 27
ROWS = [1250, 125000, 12500, 1000, 1000, 12500, 1250, 12500, 12500, 1000, 1250, 1000, 1250, 1250,
        12500, 12500, 1250, 1000, 1000, 1000, 1000, 12500, 1000, 1250, 1000, 1250, 1250]
HIDDEN1, HIDDEN2 = 512, 256
STEP = 256
STEPS = BATCH // STEP
TILES = STEP // 128

NP = 8
PICK_ROWS, PICK_PART = 1000, 125
PICK_CHUNKS = PICK_ROWS // PICK_PART
PICKED = [f for f in range(FEATURES) if ROWS[f] == PICK_ROWS][:NP]
GATHERED = [f for f in range(FEATURES) if f not in PICKED]
SLOTS = GATHERED + PICKED
NG = len(GATHERED)
HALVES = 2
PASSES = [(0, 0), (1, 0), (0, 1)]

SLOT_PAD = 32
QUADS = 4
PROD_ROWS = (QUADS - 1) * SLOT_PAD + FEATURES
GROUPS = 128 // QUADS
GROUPS_PER_USE = 8
USES = GROUPS // GROUPS_PER_USE
COLS = TILES * GROUPS

SHIFTS = FEATURES // 2
WRAP = FEATURES + SHIFTS
CHUNKS = 3
SHIFTS_PER_CHUNK = 4
CUT = FEATURES // CHUNKS
PAIRS_PER_CHUNK = SHIFTS_PER_CHUNK * FEATURES + CUT
KC1 = 1 + CHUNKS
NC1, NC2 = HIDDEN1 // 128, HIDDEN2 // 128

TURN_WIDTH = 4
TURNS = -(-NG // TURN_WIDTH)
STAGES = 4

PICKS = [("pick", n) for n in range(NP)]
TURN = [[("turn", t * TURNS + n) for n in range(TURNS)] for t in range(TILES)]
PROD = [[("prod", t * USES + u) for u in range(USES)] for t in range(TILES)]
H1, H2, Y = [("h1", n) for n in range(NC1)], [("h2", n) for n in range(NC2)], [("y", 0)]
MLP = H1 + H2 + Y
LAST_H1 = [("last_h1", c) for c in range(KC1)]


def woven(a, b, lead):
    out, a, b = a[:lead], list(a[lead:]), list(b)
    while a or b:
        out = out + b[:1] + a[:1]
        a, b = a[1:], b[1:]
    return out


OPENING, SECOND, INNER, CLOSING, AFTER = "opening", "second", "inner", "closing", "after"
ORDER = {
    OPENING: (woven(PICKS, TURN[0] + TURN[1][:1], 2) + TURN[1][1:2] + PROD[0][:2] + TURN[1][2:3] + PROD[0][2:]
              + TURN[1][3:] + PROD[1]),
    SECOND: (woven(PICKS, TURN[0], 1) + TURN[1][:1] + PROD[0] + TURN[1][1:2] + H1[:1] + TURN[1][2:3] + H1[1:3]
             + TURN[1][3:4] + H1[3:] + TURN[1][4:] + H2 + PROD[1][:1] + Y + PROD[1][1:]),
    INNER: (woven(PICKS, TURN[0] + TURN[1][:1], 1) + TURN[1][1:2] + PROD[0] + woven(H1[:3], TURN[1][2:], 1) + H1[3:]
            + PROD[1][:1] + H2 + PROD[1][1:2] + Y + PROD[1][2:]),
    CLOSING: (woven(PICKS, TURN[0] + TURN[1][:1], 1) + TURN[1][1:2] + woven(PROD[0], TURN[1][2:], 1) + PROD[1]
              + H1 + H2 + LAST_H1[:2] + Y + LAST_H1[2:]),
    AFTER: H2 + Y,
}
SHARED = ("pick", "h1", "h2", "y")


def turn_width(q):
    return min(TURN_WIDTH, NG - TURN_WIDTH * (q % TURNS))


def shared_place(kind, item):
    return [x for x in ORDER[kind] if x[0] in SHARED].index(item)


PAIR_READS = [[(r * FEATURES, SHIFTS_PER_CHUNK * c + r + 1, 0, FEATURES) for r in range(SHIFTS_PER_CHUNK)]
              + [(SHIFTS_PER_CHUNK * FEATURES, SHIFTS, CUT * c, CUT)] for c in range(CHUNKS)]
READS_PER_CHUNK = len(PAIR_READS[0])
BY_POOL = 1
ALL_TILES = list(range(TILES))


def pair_rows():
    def row(i, k):
        a, b = SLOTS[i], SLOTS[(i + k) % FEATURES]
        hi, lo = max(a, b), min(a, b)
        return DIM + hi * (hi - 1) // 2 + lo
    rows = []
    for c in range(CHUNKS):
        for k in range(SHIFTS_PER_CHUNK * c + 1, SHIFTS_PER_CHUNK * (c + 1) + 1):
            rows += [row(i, k) for i in range(FEATURES)]
        rows += [row(i, SHIFTS) for i in range(CUT * c, CUT * (c + 1))]
    return rows


def build(nc, gather_ids, pick_ids, bottom_t, tables, w_bottom, w_pairs, b1, w2, b2, w3, out):
    fp32, f32r, i32 = mybir.dt.float32, mybir.dt.float32r, mybir.dt.int32
    ALU, ACT = mybir.AluOpType, mybir.ActivationFunctionType

    ctx = ExitStack()
    with ctx:
        def sb(name, shape, dt):
            return ctx.enter_context(nc.sbuf_tensor(name, shape, dt))

        def pb(name, shape, dt):
            return ctx.enter_context(nc.psum_tensor(name, shape, dt))

        def sem(name):
            return ctx.enter_context(nc.semaphore(name))

        gids_all = sb("gids_all", [128, STEPS, TILES * NG], i32)
        gids = [sb(f"gids{p}", [128, TILES * NG], i32) for p in range(2)]
        rows = sb("rows", [128, 2, TILES, NG * DIM], fp32)
        features = sb("features", [128, TILES, GROUPS, QUADS, SLOT_PAD], fp32)
        pids = sb("pids", [128, NP, STEP], i32)
        onehot = sb("onehot", [128, 2, PICK_CHUNKS, STEP], f32r)
        halves = sb("halves", [128, NP, HALVES, PICK_CHUNKS * DIM], f32r)
        products = sb("products", [128, FEATURES, COLS], fp32)
        x1 = sb("x1", [128, KC1, STEP], fp32)
        x1_half = [sb(f"x1_half{h}", [128, KC1, STEP], f32r) for h in range(HALVES)]
        w1_half = [sb(f"w1_half{h}", [128, KC1, HIDDEN1], f32r) for h in range(HALVES)]
        w2_sb = sb("w2_sb", [128, NC1, HIDDEN2], fp32)
        w3_sb = sb("w3_sb", [128, NC2], fp32)
        b1_sb = sb("b1_sb", [128, NC1], fp32)
        b2_sb = sb("b2_sb", [128, NC2], fp32)
        hid1 = sb("hid1", [128, NC1, STEP], fp32)
        hid2 = sb("hid2", [128, NC2, STEP], fp32)
        weighted = sb("weighted", [128, STEP], fp32)
        ones = sb("ones", [128, 1], fp32)
        y_sb = sb("y_sb", [1, STEP], fp32)
        ident = sb("ident", [128, 128], fp32)
        row_id_i = sb("row_id_i", [128, PICK_CHUNKS], i32)
        row_id = sb("row_id", [128, PICK_CHUNKS], fp32)

        table_size = PICK_CHUNKS * DIM
        staged = [rows[0:PICK_PART, 1, n // 2, n % 2 * table_size:(n % 2 + 1) * table_size] for n in range(STAGES)]
        w1_staged = [hid1[:, n * HIDDEN1 // STEP:(n + 1) * HIDDEN1 // STEP, :].rearrange("p a b -> p (a b)")
                     for n in range(2)]

        turned = [pb(f"turned{n}", [128, TURN_WIDTH, 128], fp32) for n in range(2)]
        prods = [pb(f"prods{n}", [128, GROUPS_PER_USE, 128], fp32) for n in range(2)]
        last_h1 = [prods[n // 2][:, n % 2 * 4:n % 2 * 4 + TILES, :].rearrange("p a b -> p (a b)") for n in range(NC1)]
        shared = [pb(f"shared{n}", [128, 512], fp32) for n in range(2)]

        scratch = nc.dram_tensor("scratch", (128, WRAP, COLS), fp32, kind="Internal").ap()

        gids_loaded = sem("gids_loaded")
        gids_copied = sem("gids_copied")
        carried = sem("carried")
        pids_loaded = sem("pids_loaded")
        bottom_loaded = sem("bottom_loaded")
        table_loaded = [sem(f"table_loaded{n}") for n in range(STAGES)]
        weights_loaded = sem("weights_loaded")
        w1_loaded = [sem(f"w1_loaded{n}") for n in range(2)]
        w1_added = sem("w1_added")
        w1_split = sem("w1_split")
        w1_high = sem("w1_high")
        x1_high = sem("x1_high")
        x1_split = sem("x1_split")
        ident_zero = sem("ident_zero")
        ident_ready = sem("ident_ready")
        iota_ready = sem("iota_ready")
        consts_ready = sem("consts_ready")
        padded = sem("padded")
        high_ready = sem("high_ready")
        low_ready = sem("low_ready")
        gathered = [[sem(f"gathered{p}{q}") for q in range(TILES * TURNS)] for p in range(2)]
        onehot_ready = sem("onehot_ready")
        weighted_first = sem("weighted_first")
        weighted_ready = sem("weighted_ready")
        shared_full = sem("shared_full")
        shared_free = sem("shared_free")
        turned_full = sem("turned_full")
        turned_free = sem("turned_free")
        prods_full = sem("prods_full")
        prods_free = sem("prods_free")
        scratch_written = sem("scratch_written")
        pairs_loaded = sem("pairs_loaded")
        last_scratch_written = sem("last_scratch_written")
        last_pairs_loaded = [[sem(f"last_pairs_loaded{t}{c}") for c in range(CHUNKS)] for t in range(TILES)]
        last_h1_full = sem("last_h1_full")
        last_h1_free = sem("last_h1_free")
        y_stored = sem("y_stored")

        def of_tiles(cols, tiles):
            return cols.rearrange("d (g t m) -> d g t m", g=QUADS, t=TILES)[:, :, tiles[0]:tiles[-1] + 1, :]

        def tile_block(rows_of, n_rows, tiles):
            flat = rows_of.rearrange("p j c -> p (j c)")
            cols = len(tiles) * GROUPS
            start = tiles[0] * GROUPS * n_rows
            return flat[:, start:start + n_rows * cols].rearrange("p (j c) -> p j c", j=n_rows)

        PAIR_LOADS = CHUNKS * READS_PER_CHUNK
        WEIGHT_LOADS = 4

        def first(s):
            return type(s) is int and s == 0

        def shared_before(s):
            return 0 if first(s) else s * (NP + len(MLP)) - len(MLP)

        def shared_bank(s, par, place):
            return shared[place % 2 if first(s) else (par * (NP + len(MLP)) + len(MLP) + place) % 2]

        def write_scratch(queue, tiles, written):
            src, dst = tile_block(products, FEATURES, tiles), tile_block(scratch, WRAP, tiles)
            queue.dma_start(dst[:, 0:FEATURES, :], src).then_inc(written, 16)
            queue.dma_start(dst[:, FEATURES:WRAP, :], src[:, 0:SHIFTS, :]).then_inc(written, 16)

        def read_scratch(queue, tiles, c, loaded):
            cols = len(tiles) * GROUPS
            by_quad = scratch.rearrange("(g i) j c -> g (i j c)", g=QUADS)
            one_on = WRAP * COLS + cols
            for part, shift, i0, n in PAIR_READS[c]:
                start = tiles[0] * GROUPS * WRAP + i0 * one_on + shift * cols
                src = by_quad[:, start:start + n * one_on].rearrange("g (i x) -> i g x", i=n)[:, :, 0:cols]
                dst = of_tiles(x1[part:part + n, 1 + c, :], tiles).rearrange("q g t m -> q g (t m)")
                queue.dma_start(dst, src).then_inc(loaded, 16)

        def run_steps(engine, body):
            body(0, 0, OPENING)
            body(1, 1, SECOND)
            body(2, 0, INNER)
            with engine.Fori(1, (STEPS - 2) // 2) as i:
                body(i * 2 + 1, 1, INNER)
                body(i * 2 + 2, 0, INNER)
            body(STEPS - 1, 1, CLOSING)

        block = ctx.enter_context(nc.Block())

        @block.gpsimd
        def _(pool):
            nc.gpsimd.memset(ident[:, :], 0.0).then_inc(ident_zero, 1)
            nc.gpsimd.iota(row_id_i[:, :], pattern=[[1, PICK_CHUNKS]], base=0,
                           channel_multiplier=PICK_CHUNKS).then_inc(iota_ready, 1)
            pool.wait_ge(ident_zero, 1)
            nc.gpsimd.affine_select(out=ident[:, :], in_=ident[:, :], compare_op=ALU.not_equal, fill=1.0,
                                    base=0, pattern=[[-1, 128]], channel_multiplier=1).then_inc(ident_ready, 1)
            pool.wait_ge(gids_loaded, 16)
            nc.gpsimd.tensor_copy(gids[0][:, :], gids_all[:, 0, :]).then_inc(gids_copied, 1)

            def step(s, par, k, last=False):
                pool.wait_ge(gids_copied, s + 1)
                pool.sem_inc(carried, 1)
                for t in range(TILES):
                    if not k_is_0(k):
                        pool.wait_ge(turned_full, (s - 2) * (TILES * TURNS) + (t + 1) * TURNS)
                        pool.sem_inc(carried, 1)
                    elif par == 1:
                        pool.wait_ge(low_ready, NP)
                    for g, f in enumerate(GATHERED):
                        pool.indirect_dma_start(
                            rows[:, par, t, g * DIM:(g + 1) * DIM], None, tables[f][:, :],
                            bass.IndirectOffsetOnAxis(ap=gids[par][:, t * NG + g:t * NG + g + 1], axis=0),
                        ).then_inc(gathered[par][t * TURNS + g // TURN_WIDTH], 16)
                    if t == 0 and not last:
                        if not (k_is_0(k) and par == 0):
                            for q in range(TILES * TURNS):
                                pool.wait_ge(gathered[1 - par][q], 16 * turn_width(q) * (k + par))
                            pool.sem_inc(carried, 1)
                        nc.gpsimd.tensor_copy(gids[1 - par][:, :], gids_all[:, s + 1, :]).then_inc(gids_copied, 1)

            def k_is_0(k):
                return type(k) is int and k == 0

            step(0, 0, 0)
            step(1, 1, 0)
            with pool.Fori(1, STEPS // 2 - 1) as i:
                step(i * 2, 0, i)
                step(i * 2 + 1, 1, i)
            step(STEPS - 2, 0, STEPS // 2 - 1)
            step(STEPS - 1, 1, STEPS // 2 - 1, last=True)
            pool.wait_ge(x1_split, STEPS - 1)
            for t in range(TILES):
                if t == 0:
                    pool.wait_ge(scratch_written, STEPS * 32)
                else:
                    pool.wait_ge(last_scratch_written, 32)
                read_scratch(pool, [t], BY_POOL, last_pairs_loaded[t][BY_POOL])

        @block.sync
        def _(sp):
            def load_pids(s):
                sp.dma_start(pids[:, :, :], pick_ids[s, :, :].partition_broadcast(128)).then_inc(pids_loaded, 16)

            def load_bottom(s):
                sp.dma_start(x1[:, 0, :], bottom_t[s, :, :]).then_inc(bottom_loaded, 16)

            def store_y(s):
                sp.dma_start(out[s, :, :], y_sb[:, :]).then_inc(y_stored, 16)

            def finish_y(s, kind):
                sp.wait_ge(shared_free, shared_before(s) + shared_place(kind, Y[0]) + 1)
                store_y(s - 1)
                sp.wait_ge(y_stored, s * 16)

            sp.dma_start(gids_all[:, :, :], gather_ids[:, :, :]).then_inc(gids_loaded, 16)
            load_pids(0)
            for n, f in enumerate(PICKED):
                if n >= STAGES:
                    sp.wait_ge(low_ready, n - STAGES + 1)
                sp.dma_start(staged[n % STAGES], tables[f].rearrange("(p c) d -> p (c d)", p=PICK_PART)
                             ).then_inc(table_loaded[n % STAGES], 16)

            sp.dma_start(w1_staged[0], w_bottom[0, :, :]).then_inc(w1_loaded[0], 16)
            sp.dma_start(w1_staged[1], w_bottom[1, :, :]).then_inc(w1_loaded[1], 16)
            for c in range(CHUNKS):
                if c == 0:
                    sp.wait_ge(w1_added, 1)
                else:
                    sp.wait_ge(w1_split, c)
                sp.dma_start(w1_staged[(c + 1) % 2][0:PAIRS_PER_CHUNK, :], w_pairs[c, :, :]
                             ).then_inc(w1_loaded[(c + 1) % 2], 16)

            def to_scratch(s, tiles=ALL_TILES):
                sp.wait_ge(prods_free, s * (TILES * USES) + (tiles[-1] + 1) * USES)
                write_scratch(sp, tiles, scratch_written)
                sp.wait_ge(scratch_written, s * 32 + 32)

            def step(s, par, kind):
                if kind != CLOSING:
                    sp.wait_ge(onehot_ready, s * NP + NP)
                    load_pids(s + 1)
                if kind in (SECOND, INNER):
                    finish_y(s, kind)
                elif kind == CLOSING:
                    sp.wait_ge(x1_split, s)
                load_bottom(s)
                if kind != CLOSING:
                    to_scratch(s)
                    for c in range(CHUNKS):
                        read_scratch(sp, ALL_TILES, c, pairs_loaded)
                else:
                    to_scratch(s, [0])
                    for t in range(TILES):
                        if t == 1:
                            sp.wait_ge(last_scratch_written, 32)
                        for c in range(CHUNKS):
                            if c != BY_POOL:
                                read_scratch(sp, [t], c, last_pairs_loaded[t][c])
                    finish_y(s, kind)

            run_steps(sp, step)
            sp.wait_ge(shared_free, shared_before(STEPS) + len(ORDER[AFTER]))
            store_y(STEPS - 1)
            sp.wait_ge(y_stored, 16 * STEPS)

        @block.scalar
        def _(act):
            def load_weights():
                act.dma_start(w2_sb[:, :, :], w2.rearrange("(c p) n -> p c n", p=128)).then_inc(weights_loaded, 16)
                act.dma_start(w3_sb[:, :], w3[:, :]).then_inc(weights_loaded, 16)
                act.dma_start(b1_sb[:, :], b1[:, :]).then_inc(weights_loaded, 16)
                act.dma_start(b2_sb[:, :], b2[:, :]).then_inc(weights_loaded, 16)

            def high_half(n):
                act.wait_ge(table_loaded[n % STAGES], 16 * (n // STAGES + 1))
                nc.scalar.copy(halves[0:PICK_PART, n, 0, :], staged[n % STAGES]).then_inc(high_ready, 1)

            for n in range(STAGES):
                high_half(n)
                if n == 0:
                    load_weights()

            def copy_shared(s, par, kind, item):
                what, n = item
                place = shared_place(kind, item)
                src = shared_bank(s, par, place)[:, 0:STEP]
                act.wait_ge(shared_full, shared_before(s) + place + 1)
                if item == H1[0]:
                    act.wait_ge(weights_loaded, 16 * WEIGHT_LOADS)
                    act.wait_ge(w1_split, KC1)
                if what == "pick":
                    ins = nc.scalar.copy(features[:, :, :, :, NG + n].rearrange("d t m g -> d g t m"),
                                         src.rearrange("d (g t m) -> d g t m", g=QUADS, t=TILES))
                elif what == "h1":
                    ins = nc.scalar.activation(hid1[:, n, :], src, ACT.Relu, bias=b1_sb[:, n:n + 1])
                elif what == "h2":
                    ins = nc.scalar.activation(hid2[:, n, :], src, ACT.Relu, bias=b2_sb[:, n:n + 1])
                else:
                    if kind == AFTER:
                        act.wait_ge(y_stored, 16 * (STEPS - 1))
                    ins = nc.scalar.copy(y_sb[0:1, :], src[0:1, :])
                ins.then_inc(shared_free, 1)

            def copy_turned(s, q):
                t, n = divmod(q, TURNS)
                act.wait_ge(turned_full, s * (TILES * TURNS) + q + 1)
                width = turn_width(q)
                dst = features[:, t, :, :, TURN_WIDTH * n:TURN_WIDTH * n + width].rearrange("d m g f -> d g m f")
                nc.scalar.copy(dst, turned[q % 2][:, 0:width, :].rearrange("d f (g m) -> d g m f", g=QUADS)
                               ).then_inc(turned_free, 1)

            def copy_products(s, q, kind):
                t, u = divmod(q, USES)
                if q == 0 and first(s):
                    act.wait_ge(padded, 1)
                elif q == 0:
                    act.wait_ge(scratch_written, s * 32)
                act.wait_ge(prods_full, s * (TILES * USES) + q + 1)
                if kind == CLOSING:
                    dst, m0 = tile_block(products, FEATURES, [t]), GROUPS_PER_USE * u
                else:
                    dst, m0 = products, t * GROUPS + GROUPS_PER_USE * u
                for g in range(QUADS):
                    quad = slice(SLOT_PAD * g, min(SLOT_PAD * (g + 1), PROD_ROWS))
                    last = nc.scalar.copy(dst[quad, :, m0:m0 + GROUPS_PER_USE].rearrange("p j m -> p m j"),
                                          prods[q % 2][quad, :, FEATURES * g:FEATURES * (g + 1)])
                last.then_inc(prods_free, 1)
                if kind == CLOSING and q == TILES * USES - 1:
                    act.wait_ge(prods_free, STEPS * (TILES * USES))
                    act.wait_ge(pairs_loaded, s * (16 * PAIR_LOADS))
                    write_scratch(act, [t], last_scratch_written)

            def copy_last_h1():
                for n in range(NC1):
                    act.wait_ge(last_h1_full, n + 1)
                    nc.scalar.activation(hid1[:, n, :], last_h1[n], ACT.Relu,
                                         bias=b1_sb[:, n:n + 1]).then_inc(last_h1_free, 1)

            def step(s, par, kind):
                for item in ORDER[kind]:
                    if item[0] == "turn":
                        copy_turned(s, item[1])
                    elif item[0] == "prod":
                        copy_products(s, item[1], kind)
                    elif item[0] == "last_h1":
                        if item == LAST_H1[-1]:
                            copy_last_h1()
                    else:
                        if kind == OPENING and item[1] + STAGES < NP:
                            high_half(item[1] + STAGES)
                        copy_shared(s, par, kind, item)

            run_steps(act, step)
            step(STEPS, 0, AFTER)

        @block.vector
        def _(dve):
            nc.vector.memset(features[:, :, :, :, FEATURES:SLOT_PAD], 0.0)
            nc.vector.memset(ones[:, :], 1.0)
            nc.vector.memset(products[SLOT_PAD * (QUADS - 1):, :, :], 0.0).then_inc(padded, 1)
            dve.wait_ge(iota_ready, 1)
            nc.vector.tensor_copy(row_id[:, :], row_id_i[:, :]).then_inc(consts_ready, 1)
            dve.wait_ge(consts_ready, 1)

            def low_half(n):
                dve.wait_ge(high_ready, n + 1)
                nc.vector.tensor_tensor(halves[0:PICK_PART, n, 1, :], staged[n % STAGES],
                                        halves[0:PICK_PART, n, 0, :].bitcast(fp32),
                                        ALU.subtract).then_inc(low_ready, 1)

            def split_w1():
                for c in range(KC1):
                    used = slice(0, DIM if c == 0 else PAIRS_PER_CHUNK)
                    here = w1_staged[c % 2][used, :]
                    if c == 0:
                        for n in range(2):
                            dve.wait_ge(w1_loaded[n], 16)
                        nc.vector.tensor_tensor(here, here, w1_staged[1], ALU.add).then_inc(w1_added, 1)
                        dve.wait_ge(w1_added, 1)
                    else:
                        dve.wait_ge(w1_loaded[c % 2], 16 * (c // 2 + 1 + c % 2))
                    nc.vector.tensor_copy(w1_half[0][used, c, :], here).then_inc(w1_high, 1)
                    dve.wait_ge(w1_high, c + 1)
                    nc.vector.tensor_tensor(w1_half[1][used, c, :], here, w1_half[0][used, c, :].bitcast(fp32),
                                            ALU.subtract).then_inc(w1_split, 1)

            def split_x1(chunks, tiles, splits):
                parts = []
                for c in chunks:
                    used = slice(0, DIM if c == 0 else PAIRS_PER_CHUNK)
                    parts.append([of_tiles(x[used, c, :], tiles) for x in (x1, x1_half[0], x1_half[1])])
                for whole, high, low in parts:
                    last = nc.vector.tensor_copy(high, whole)
                last.then_inc(x1_high, 1)
                dve.wait_ge(x1_high, splits + 1)
                for whole, high, low in parts:
                    last = nc.vector.tensor_tensor(low, whole, high.bitcast(fp32), ALU.subtract)
                last.then_inc(x1_split, 1)

            def weigh(s, kind):
                for n in range(NC2):
                    dve.wait_ge(shared_free, shared_before(s) + shared_place(kind, H2[n]) + 1)
                    if n == 0:
                        if kind == SECOND:
                            dve.wait_ge(weights_loaded, 16 * WEIGHT_LOADS)
                        nc.vector.tensor_scalar(weighted[:, :], hid2[:, 0, :], w3_sb[:, 0:1], None,
                                                ALU.mult).then_inc(weighted_first, 1)
                    else:
                        dve.wait_ge(weighted_first, s)
                        nc.vector.scalar_tensor_tensor(weighted[:, :], hid2[:, 1, :], w3_sb[:, 1:2], weighted[:, :],
                                                       ALU.mult, ALU.add).then_inc(weighted_ready, 1)

            def step(s, par, kind):
                dve.wait_ge(pids_loaded, s * 16 + 16)
                for n in range(NP):
                    if n >= 2:
                        if kind == OPENING:
                            low_half(n)
                        dve.wait_ge(shared_full, shared_before(s) + shared_place(kind, PICKS[n - 2]) + 1)
                    elif n == 0 and kind != OPENING:
                        dve.wait_ge(prods_full, (s - 1) * (TILES * USES) + 1)
                    for c in range(PICK_CHUNKS):
                        last = nc.vector.tensor_scalar(onehot[0:PICK_PART, (par * NP + n) % 2, c, :],
                                                       pids[0:PICK_PART, n, :],
                                                       row_id[0:PICK_PART, c:c + 1], None, ALU.is_equal)
                    last.then_inc(onehot_ready, 1)
                    if kind == OPENING and n == 1:
                        low_half(0)
                        low_half(1)
                if kind == OPENING:
                    split_w1()
                else:
                    dve.wait_ge(bottom_loaded, s * 16)
                    dve.wait_ge(pairs_loaded, s * (16 * PAIR_LOADS))
                    split_x1(range(KC1), ALL_TILES, s - 1)
                    if kind != CLOSING:
                        weigh(s, kind)

            run_steps(dve, step)
            dve.wait_ge(shared_full, shared_before(STEPS - 1) + shared_place(CLOSING, H1[-1]) + 1)
            dve.wait_ge(bottom_loaded, STEPS * 16)
            split_x1([0], ALL_TILES, STEPS - 1)
            for c in range(CHUNKS):
                dve.wait_ge(last_pairs_loaded[0][c], 16 * READS_PER_CHUNK)
            split_x1(range(1, KC1), [0], STEPS)
            for c in range(CHUNKS):
                dve.wait_ge(last_pairs_loaded[1][c], 16 * READS_PER_CHUNK)
                split_x1([1 + c], [1], STEPS + 1 + c)
                if c == 0:
                    weigh(STEPS - 1, CLOSING)
            weigh(STEPS, AFTER)

        @block.tensor
        def _(pe):
            pe.wait_ge(ident_ready, 1)

            def pick(s, par, n, dst):
                pe.wait_ge(onehot_ready, s * NP + n + 1)
                if first(s):
                    pe.wait_ge(low_ready, n + 1)
                for half in range(HALVES):
                    for c in range(PICK_CHUNKS):
                        last = nc.tensor.matmul(dst, halves[0:PICK_PART, n, half, c * DIM:(c + 1) * DIM],
                                                onehot[0:PICK_PART, (par * NP + n) % 2, c, :],
                                                start=(half == 0 and c == 0),
                                                stop=(half == HALVES - 1 and c == PICK_CHUNKS - 1))
                return last

            def layer1_chunk(n, c, dst):
                used = slice(0, DIM if c == 0 else PAIRS_PER_CHUNK)
                for wh, xh in PASSES:
                    last = nc.tensor.matmul(dst, w1_half[wh][used, c, 128 * n:128 * n + 128], x1_half[xh][used, c, :],
                                            start=(c == 0 and (wh, xh) == PASSES[0]),
                                            stop=(c == KC1 - 1 and (wh, xh) == PASSES[-1]))
                return last

            def layer1(s, n, dst):
                if n == 0:
                    pe.wait_ge(w1_split, KC1)
                    pe.wait_ge(x1_split, s)
                for c in range(KC1):
                    last = layer1_chunk(n, c, dst)
                return last

            def last_layer1(c):
                if c == 0:
                    pe.wait_ge(prods_free, STEPS * (TILES * USES))
                pe.wait_ge(x1_split, STEPS if c == 0 else STEPS + 1 + c)
                for n in range(NC1):
                    last = layer1_chunk(n, c, last_h1[n])
                    if c == KC1 - 1:
                        last.then_inc(last_h1_full, 1)

            def layer2(n, kind, dst):
                for c in range(NC1):
                    if kind == AFTER and n == 0:
                        pe.wait_ge(last_h1_free, c + 1)
                    last = nc.tensor.matmul(dst, w2_sb[:, c, 128 * n:128 * n + 128], hid1[:, c, :],
                                            start=(c == 0), stop=(c == NC1 - 1))
                return last

            def fill_shared(s, par, kind, item):
                what, n = item
                place = shared_place(kind, item)
                dst = shared_bank(s, par, place)[:, 0:STEP]
                if not (first(s) and place < 2):
                    pe.wait_ge(shared_free, shared_before(s) + place - 1)
                if what == "pick":
                    last = pick(s, par, n, dst)
                elif what == "h1":
                    last = layer1(s, n, dst)
                elif what == "h2":
                    if kind != AFTER:
                        pe.wait_ge(shared_free, shared_before(s) + shared_place(kind, H1[-1]) + 1)
                    last = layer2(n, kind, dst)
                else:
                    pe.wait_ge(weighted_ready, s)
                    last = nc.tensor.matmul(dst[0:1, :], ones[:, :], weighted[:, :], start=True, stop=True)
                last.then_inc(shared_full, 1)

            def transpose_rows(s, par, q):
                t, n = divmod(q, TURNS)
                pe.wait_ge(gathered[par][q], (s - par) * (8 * turn_width(q)) + 16 * turn_width(q))
                if not (first(s) and q < 2):
                    pe.wait_ge(turned_free, s * (TILES * TURNS) + q - 1)
                for j in range(turn_width(q)):
                    g = TURN_WIDTH * n + j
                    last = nc.tensor.transpose(turned[q % 2][:, j, :], rows[:, par, t, g * DIM:(g + 1) * DIM],
                                               ident[:, :])
                last.then_inc(turned_full, 1)

            def pair_products(s, kind, q):
                t, u = divmod(q, USES)
                if u == 0:
                    pe.wait_ge(turned_free, s * (TILES * TURNS) + (t + 1) * TURNS)
                    if t == 0:
                        pe.wait_ge(shared_free, shared_before(s) + shared_place(kind, PICKS[-1]) + 1)
                if not (first(s) and q < 2):
                    pe.wait_ge(prods_free, s * (TILES * USES) + q - 1)
                for j in range(GROUPS_PER_USE):
                    group = features[:, t, GROUPS_PER_USE * u + j, :, :]
                    last = nc.tensor.matmul(prods[q % 2][0:PROD_ROWS, j, 0:QUADS * FEATURES],
                                            group.rearrange("d g f -> d (g f)")[:, 0:PROD_ROWS],
                                            group[:, :, 0:FEATURES], start=True, stop=True)
                last.then_inc(prods_full, 1)

            def step(s, par, kind):
                for item in ORDER[kind]:
                    if item[0] == "turn":
                        transpose_rows(s, par, item[1])
                    elif item[0] == "prod":
                        pair_products(s, kind, item[1])
                    elif item[0] == "last_h1":
                        last_layer1(item[1])
                    else:
                        fill_shared(s, par, kind, item)

            run_steps(pe, step)
            step(STEPS, 0, AFTER)


def kernel(**inputs):
    import numpy as np
    import concourse.bacc as bacc
    from concourse.bass_utils import run_bass_kernel_spmd

    a = {name: np.asarray(x) for name, x in inputs.items()}
    ids, w1 = a["ids"], a["W_top1"]

    def in_product_order(x):
        return x.reshape(STEPS, TILES, QUADS, GROUPS, -1).transpose(0, 2, 1, 3, 4).reshape(STEPS, STEP, -1)

    laid = {
        "gather_ids": ids[:, GATHERED].reshape(STEPS, TILES, 128, NG).transpose(2, 0, 1, 3)
                      .reshape(128, STEPS, TILES * NG),
        "pick_ids": in_product_order(ids[:, PICKED]).transpose(0, 2, 1),
        "bottom_t": in_product_order(a["r_bottom_mlp_out"]).transpose(0, 2, 1),
        "w_bottom": np.stack([w1[:DIM], w1[-DIM:]]),
        "w_pairs": w1[pair_rows()].reshape(CHUNKS, PAIRS_PER_CHUNK, HIDDEN1),
        "b1": a["b_top1"].reshape(NC1, 128).T,
        "w2": a["W_top2"],
        "b2": a["b_top2"].reshape(NC2, 128).T,
        "w3": a["W_top3"].reshape(NC2, 128).T,
    }
    laid.update({f"tbl_{f}": a[f"tbl_{f}"] for f in range(FEATURES)})
    laid = {name: np.ascontiguousarray(x) for name, x in laid.items()}

    nc = bacc.Bacc("TRN2", target_bir_lowering=False, num_devices=1)
    ap = {name: nc.dram_tensor(f"in_{name}", x.shape, mybir.dt.from_np(x.dtype), kind="ExternalInput").ap()
          for name, x in laid.items()}
    out = nc.dram_tensor("out_y", (STEPS, 1, STEP), mybir.dt.float32, kind="ExternalOutput").ap()
    build(nc, ap["gather_ids"], ap["pick_ids"], ap["bottom_t"], [ap[f"tbl_{f}"] for f in range(FEATURES)],
          ap["w_bottom"], ap["w_pairs"], ap["b1"], ap["w2"], ap["b2"], ap["w3"], out)
    r = run_bass_kernel_spmd(nc, [{f"in_{name}": x for name, x in laid.items()}], core_ids=[0])
    y = r.results[0]["out_y"].reshape(STEPS, QUADS, TILES, GROUPS)
    return y.transpose(0, 2, 1, 3).reshape(BATCH, 1)
```
